# Optimizing a Trainium2 kernel written in Bass

```python
import numpy as np
import jax
import jax.numpy as jnp

def _softmax(x, axis=-1):
    return jax.nn.softmax(x, axis=axis)

def _gelu(x):
    return jax.nn.gelu(x, approximate=True)

def _silu(x):
    return jax.nn.silu(x)

def _sigmoid(x):
    return jax.nn.sigmoid(x)

def _layernorm(x, axis=-1, eps=1e-05):
    m = jnp.mean(x, axis=axis, keepdims=True)
    v = jnp.var(x, axis=axis, keepdims=True)
    return (x - m) / jnp.sqrt(v + eps)

def _scatter_add(tgt, idx, src, axis=0):
    return tgt.at[idx].add(src)

def _segment_sum(src, seg, n):
    return jax.ops.segment_sum(src, seg, n)
kernel_name = 'mk_adj_resnorm_d1_adj_r2_59a106'

def setup_inputs(seed: int=0):
    np.random.seed(seed)
    _w = jnp.asarray

    def _rec_inputs():
        import jax
        import jax.numpy as jnp
        _gk = jax.random.key(seed)
        x = -0.000929 + 1 * jax.random.normal(jax.random.fold_in(_gk, 1), (8192, 64), jnp.float32)
        _a = jax.random.bernoulli(jax.random.fold_in(_gk, 2), 0.000488281, (8192, 8192))
        _a = jnp.logical_or(_a, jnp.swapaxes(_a, -1, -2))
        _a = jnp.logical_or(_a, jnp.eye(8192, dtype=bool))
        _af = _a.astype(jnp.float32)
        _af = _af * jax.random.uniform(jax.random.fold_in(_gk, 3), (8192, 8192), jnp.float32, 0.05, 6.10351e-05)
        adj = _af
        return (x, adj)
    x, adj = _rec_inputs()

    def _L0_gnn_setup():
        import jax, jax.numpy as jnp
        import numpy as np
        N, D = (8192, 64)
        key = jax.random.key(seed)
        k1, k2, k3, k4 = jax.random.split(key, 4)
        X = jax.random.normal(k1, (N, D), dtype=jnp.float32)
        A_hat = jax.random.uniform(k2, (N, N), dtype=jnp.float32) / N
        w = jax.random.uniform(k3, (N,), dtype=jnp.float32)
        W_agg = jax.random.normal(k4, (D, D), dtype=jnp.float32) * (1.0 / np.sqrt(D))
        return {'X': X, 'A_hat': A_hat, 'w': w, 'W_agg': W_agg}
    _L0_gnn_all = _L0_gnn_setup()
    _L0_gnn_in = {k: v for k, v in _L0_gnn_all.items() if k in ('w', 'W_agg')}
    del _L0_gnn_all
    return {'x': x, 'adj': adj, 'L0_gnn_w': _L0_gnn_in['w'], 'L0_gnn_W_agg': _L0_gnn_in['W_agg']}

def reference(x, adj, L0_gnn_w, L0_gnn_W_agg):
    import jax
    import jax.numpy as jnp

    def _L0_gnn_ref(X, A_hat, w, W_agg):
        import jax, jax.numpy as jnp
        import numpy as np
        N, D = (8192, 64)
        agg = A_hat @ (X @ W_agg)
        aggregated_term = w[:, None] * jax.nn.relu(agg)
        residual_term = (1.0 - w)[:, None] * X
        return aggregated_term + residual_term
    x = _layernorm(x + _L0_gnn_ref(x, adj, L0_gnn_w, L0_gnn_W_agg), axis=-1)
    return x

_drawn_inputs = setup_inputs


def setup_inputs(seed=0):
    import zlib

    import numpy as np

    out = dict(_drawn_inputs(seed))
    spreads = {}
    factors = {}
    for name, (base, spread) in spreads.items():
        noise = np.random.default_rng([zlib.crc32(name.encode()), seed]).standard_normal(out[name].shape)
        drawn = base * np.exp(spread * noise) if base else spread * noise
        out[name] = jnp.asarray(drawn.astype(out[name].dtype))
    for name, factor in factors.items():
        out[name] = (out[name] * factor).astype(out[name].dtype)
    return out
```

```python
import concourse.bass as bass
from concourse import mybir
from contextlib import ExitStack

P = 128
D = 64
EPS = 1e-5
HALVES = 2
MAIN_SLOTS = 8
MID_SLOTS = 6
LAST_SLOTS = 2
SUB = 4
LAST_LOADS = (16, 16, 16, 8, 4, 4)
RING = 8
X_PARTS = 4


def gnn_residual_layernorm(nc, x, adj_main, adj_mid, adj_last, w, w_agg, out):
    fp32 = mybir.dt.float32
    ALU = mybir.AluOpType
    ACT = mybir.ActivationFunctionType
    AX = mybir.AxisListType

    T = x.shape[0] // P
    G, C = adj_main.shape[:2]
    MID, LAST = G, G + 1
    MID_T0 = G * MAIN_SLOTS
    LAST_T0 = MID_T0 + MID_SLOTS
    COLS = MAIN_SLOTS * P
    PAIRS = T // 2
    PB = 4
    BLOCKS = PAIRS // PB
    LOADS = (G + 1) * C + len(LAST_LOADS)
    assert C * SUB == T == sum(LAST_LOADS) and LAST_T0 + LAST_SLOTS == T and C % RING == 0

    DVE_PRE = 1
    DVE_GROUP = 9
    VSUM_STEP = 8

    def arrivals(load):
        return 16 * (load // RING + 1)

    ctx = ExitStack()
    with ctx:
        def sb(name, shape):
            return ctx.enter_context(nc.sbuf_tensor(name, shape, fp32))

        def psum(name, shape):
            return ctx.enter_context(nc.psum_tensor(name, shape, fp32))

        def sem(name):
            return ctx.enter_context(nc.semaphore(name))

        ring = sb("ring", [P, RING, SUB * COLS])
        xres = sb("xres", [P, T, D])
        xw = sb("xw", [P, T, D])
        xT = sb("xT", [P, 2, PB * P])
        w_sb = sb("w_sb", [P, T])
        one_minus_w = sb("one_minus_w", [P, T])
        wagg2 = sb("wagg2", [P, D])
        ident = sb("ident", [P, P])
        eps = sb("eps", [P, 1])
        aggT = sb("aggT", [P, COLS // HALVES])
        y = sb("y", [P, MAIN_SLOTS, D])
        sq = sb("sq", [P, MAIN_SLOTS, D])
        rowsum = sb("rowsum", [P, MAIN_SLOTS])
        varsum = sb("varsum", [P, MAIN_SLOTS])
        std = sb("std", [P, MAIN_SLOTS])
        rstd = sb("rstd", [P, MAIN_SLOTS])

        acc = psum("acc", [P, COLS // HALVES])
        rows_ps = psum("rows_ps", [P, MAIN_SLOTS * D])
        xT_ps = [psum(f"xT_ps{i}", [P, PB * P]) for i in range(2)]
        xw_ps = [[psum(f"xw_ps{i}{h}", [P, PB, D]) for h in range(2)] for i in range(2)]

        loaded = [sem(f"loaded{r}") for r in range(RING)]
        slot_free = sem("slot_free")
        x_in = [sem(f"x_in{i}") for i in range(X_PARTS)]
        w_in, wagg_in = sem("w_in"), sem("wagg_in")
        eps_ready, ident_zero, ident_ready = sem("eps_ready"), sem("ident_zero"), sem("ident_ready")
        xT_done, xT_copied = sem("xT_done"), sem("xT_copied")
        xw_done, xw_copied = sem("xw_done"), sem("xw_copied")
        agg_copied = sem("agg_copied")
        rows_done = sem("rows_done")
        dve_step = sem("dve_step")
        std_ready = sem("std_ready")
        out_ready = sem("out_ready")
        stored = sem("stored")
        block = ctx.enter_context(nc.Block())

        @block.sync
        def _(sp):
            for i in range(X_PARTS):
                part = slice(i * T // X_PARTS, (i + 1) * T // X_PARTS)
                sp.dma_start(xres[:, part], x.rearrange("(p t) d -> p t d", p=P)[:, part]).then_inc(x_in[i], 16)
                if i == 0:
                    sp.dma_start(wagg2[0:D, :], w_agg).then_inc(wagg_in, 16)
                    sp.dma_start(wagg2[D:P, :], w_agg).then_inc(wagg_in, 16)
            for c in range(C):
                if c >= RING:
                    sp.wait_ge(slot_free, c - RING + 1)
                sp.dma_start(ring[:, c % RING], adj_main[0, c].rearrange("q s n -> q (s n)")).then_inc(loaded[c % RING], 16)
            with sp.Fori(1, G) as g:
                for c in range(C):
                    sp.wait_ge(slot_free, g * C + (c - RING + 1))
                    sp.dma_start(ring[:, c % RING],
                                 adj_main[bass.ds(g, 1), c].rearrange("o q s n -> (o q) (s n)")).then_inc(loaded[c % RING], 16)
            for c in range(C):
                load = MID * C + c
                sp.wait_ge(slot_free, load - RING + 1)
                sp.dma_start(ring[:, load % RING, 0:SUB * MID_SLOTS * P],
                             adj_mid[c].rearrange("q s n -> q (s n)")).then_inc(loaded[load % RING], 16)
            j = 0
            for i, n in enumerate(LAST_LOADS):
                load = LAST * C + i
                sp.wait_ge(slot_free, load - RING + 1)
                sp.dma_start(ring[:, load % RING, 0:n * LAST_SLOTS * P],
                             adj_last[:, j:j + n].rearrange("q s n -> q (s n)")).then_inc(loaded[load % RING], 16)
                j += n

        @block.gpsimd
        def _(pool):
            nc.gpsimd.memset(ident[:], 0.0).then_inc(ident_zero, 1)
            pool.wait_ge(ident_zero, 1)
            nc.gpsimd.affine_select(out=ident[:], in_=ident[:], compare_op=ALU.not_equal, fill=1.0, base=0,
                                    pattern=[[-1, P]], channel_multiplier=1).then_inc(ident_ready, 1)
            nc.gpsimd.memset(eps[:], EPS).then_inc(eps_ready, 1)

        @block.tensor
        def _(pe):
            def transpose_x(b):
                if b % (BLOCKS // X_PARTS) == 0:
                    pe.wait_ge(x_in[b * X_PARTS // BLOCKS], 16)
                if b >= 2:
                    pe.wait_ge(xT_copied, b - 1)
                for i in range(PB):
                    t = 2 * (b * PB + i)
                    last = nc.tensor.transpose(xT_ps[b % 2][:, i * P:(i + 1) * P],
                                               xres[:, t:t + 2].rearrange("p t d -> p (t d)"), ident[:])
                last.then_inc(xT_done, 1)

            pe.wait_ge(ident_ready, 1)
            transpose_x(0)
            pe.wait_ge(wagg_in, 32)
            for b in range(BLOCKS):
                if b + 1 < BLOCKS:
                    transpose_x(b + 1)
                pe.wait_ge(xT_copied, b + 1)
                if b >= 2:
                    pe.wait_ge(xw_copied, b - 1)
                for i in range(PB):
                    for h in range(2):
                        last = nc.tensor.matmul(xw_ps[b % 2][h][:, i], xT[h * D:(h + 1) * D, b % 2, i * P:(i + 1) * P],
                                                wagg2[h * D:(h + 1) * D, :], start=True, stop=True)
                last.then_inc(xw_done, 1)
            pe.wait_ge(xw_copied, BLOCKS)

            def contract(slot, j0, n_j, n_slots):
                width = n_slots // HALVES * P
                for s in range(n_j):
                    j = j0 + s
                    for h in range(HALVES):
                        at = (s * HALVES + h) * width
                        last = nc.tensor.matmul(acc[h * D:(h + 1) * D, 0:width], xw[:, j], ring[:, slot, at:at + width],
                                                start=j == 0, stop=j == T - 1)
                last.then_inc(slot_free, 1)

            def turn_back(g, n_slots):
                pe.wait_ge(agg_copied, g + 1)
                pe.wait_ge(dve_step, g * DVE_GROUP + DVE_PRE)
                for k in range(n_slots // HALVES):
                    last = nc.tensor.transpose(rows_ps[:, k * P:(k + 1) * P], aggT[:, k * P:(k + 1) * P], ident[:])
                last.then_inc(rows_done, 1)

            with pe.Fori(0, G) as g:
                for c in range(C):
                    pe.wait_ge(loaded[c % RING], g * (16 * C // RING) + arrivals(c))
                    contract(c % RING, c * SUB, SUB, MAIN_SLOTS)
                turn_back(g, MAIN_SLOTS)
            for c in range(C):
                load = MID * C + c
                pe.wait_ge(loaded[load % RING], arrivals(load))
                contract(load % RING, c * SUB, SUB, MID_SLOTS)
            turn_back(MID, MID_SLOTS)
            j = 0
            for i, n in enumerate(LAST_LOADS):
                load = LAST * C + i
                pe.wait_ge(loaded[load % RING], arrivals(load))
                contract(load % RING, j, n, LAST_SLOTS)
                j += n
            turn_back(LAST, LAST_SLOTS)

        @block.scalar
        def _(act):
            act.wait_ge(xT_done, 1)
            act.dma_start(w_sb[:], w.rearrange("(p t) -> p t", p=P)).then_inc(w_in, 16)
            for b in range(BLOCKS):
                act.wait_ge(xT_done, b + 1)
                if b >= 2:
                    act.wait_ge(xw_done, b - 1)
                nc.scalar.copy(xT[:, b % 2], xT_ps[b % 2][:]).then_inc(xT_copied, 1)
            act.wait_ge(eps_ready, 1)

            def group(g, t0, n_slots, loads):
                width = n_slots // HALVES * P
                act.wait_ge(slot_free, loads)
                nc.scalar.copy(aggT[:, 0:width], acc[:, 0:width]).then_inc(agg_copied, 1)
                act.wait_ge(dve_step, g * DVE_GROUP + (DVE_PRE + VSUM_STEP))
                nc.scalar.activation(std[:, 0:n_slots], varsum[:, 0:n_slots], ACT.Sqrt,
                                     bias=eps[:, 0:1], scale=1.0 / D).then_inc(std_ready, 1)
                act.wait_ge(out_ready, g + 1)
                act.dma_start(out.rearrange("(p t) d -> p t d", p=P)[:, bass.ds(t0, n_slots)],
                              xres[:, bass.ds(t0, n_slots)]).then_inc(stored, 16)

            with act.Fori(0, G) as g:
                group(g, g * MAIN_SLOTS, MAIN_SLOTS, g * C + C)
            group(MID, MID_T0, MID_SLOTS, LAST * C)
            group(LAST, LAST_T0, LAST_SLOTS, LOADS)
            act.wait_ge(stored, 16 * (LAST + 1))

        @block.vector
        def _(dve):
            def step(instruction, count):
                instruction.then_inc(dve_step, 1)
                dve.wait_ge(dve_step, count)

            def over_row(v):
                return v.rearrange("p (n o) -> p n o", o=1).to_broadcast([P, v.shape[1], D])

            for b in range(BLOCKS):
                dve.wait_ge(xw_done, b + 1)
                for h in range(2):
                    last = nc.vector.tensor_copy(xw[:, 2 * PB * b + h:2 * PB * (b + 1):2], xw_ps[b % 2][h][:])
                last.then_inc(xw_copied, 1)

            dve.wait_ge(w_in, 16)
            step(nc.vector.tensor_scalar(one_minus_w[:], w_sb[:], -1.0, 1.0, ALU.mult, ALU.add), DVE_PRE)
            for i in range(X_PARTS):
                dve.wait_ge(x_in[i], 16)
            dve.wait_ge(xT_done, BLOCKS)

            def group(g, t0, n):
                base = g * DVE_GROUP + DVE_PRE
                v, s, residual = y[:, 0:n], sq[:, 0:n], xres[:, bass.ds(t0, n)]
                step(nc.vector.tensor_tensor(s, residual, over_row(one_minus_w[:, bass.ds(t0, n)]), ALU.mult), base + 1)
                step(nc.vector.tensor_tensor(residual, residual, s, ALU.add), base + 2)
                dve.wait_ge(rows_done, g + 1)
                step(nc.vector.scalar_tensor_tensor(out=v, in0=rows_ps[:, 0:n * D].rearrange("p (n d) -> p n d", d=D),
                                                    scalar=0.0, in1=over_row(w_sb[:, bass.ds(t0, n)]),
                                                    op0=ALU.max, op1=ALU.mult), base + 3)
                step(nc.vector.tensor_tensor(v, v, residual, ALU.add), base + 4)
                step(nc.vector.tensor_reduce(rowsum[:, 0:n], v, AX.X, ALU.add), base + 5)
                step(nc.vector.scalar_tensor_tensor(out=v, in0=over_row(rowsum[:, 0:n]), scalar=-1.0 / D, in1=v,
                                                    op0=ALU.mult, op1=ALU.add), base + 6)
                step(nc.vector.tensor_tensor(s, v, v, ALU.mult), base + 7)
                step(nc.vector.tensor_reduce(varsum[:, 0:n], s, AX.X, ALU.add), base + 8)
                dve.wait_ge(std_ready, g + 1)
                step(nc.vector.reciprocal(rstd[:, 0:n], std[:, 0:n]), base + 9)
                nc.vector.tensor_tensor(residual, v, over_row(rstd[:, 0:n]), ALU.mult).then_inc(out_ready, 1)

            with dve.Fori(0, G) as g:
                group(g, g * MAIN_SLOTS, MAIN_SLOTS)
            group(MID, MID_T0, MID_SLOTS)
            group(LAST, LAST_T0, LAST_SLOTS)


def kernel(x, adj, L0_gnn_w, L0_gnn_W_agg):
    import numpy as np
    import concourse.bacc as bacc
    from concourse.bass_utils import run_bass_kernel_spmd

    n = x.shape[0]
    t = n // P
    c = t // SUB
    g = (t - MID_SLOTS - LAST_SLOTS) // MAIN_SLOTS
    mid_t0 = g * MAIN_SLOTS
    last_t0 = mid_t0 + MID_SLOTS
    a = np.asarray(adj).reshape(P, t, P, t)
    main = a[:, :mid_t0].reshape(P, g, MAIN_SLOTS // HALVES, HALVES, P, c, SUB).transpose(1, 5, 4, 6, 3, 2, 0)
    mid = a[:, mid_t0:last_t0].reshape(P, MID_SLOTS // HALVES, HALVES, P, c, SUB).transpose(4, 3, 5, 2, 1, 0)
    last = a[:, last_t0:].reshape(P, LAST_SLOTS // HALVES, HALVES, P, t).transpose(3, 4, 2, 1, 0)
    arrays = {
        "x_dram": np.ascontiguousarray(x),
        "adj_main_dram": np.ascontiguousarray(main).reshape(g, c, P, SUB, MAIN_SLOTS * P),
        "adj_mid_dram": np.ascontiguousarray(mid).reshape(c, P, SUB, MID_SLOTS * P),
        "adj_last_dram": np.ascontiguousarray(last).reshape(P, t, LAST_SLOTS * P),
        "w_dram": np.ascontiguousarray(L0_gnn_w),
        "w_agg_dram": np.ascontiguousarray(L0_gnn_W_agg),
    }
    nc = bacc.Bacc("TRN2", target_bir_lowering=False, num_devices=1)
    args = [nc.dram_tensor(name, v.shape, mybir.dt.from_np(v.dtype), kind="ExternalInput").ap() for name, v in arrays.items()]
    out = nc.dram_tensor("out_dram", x.shape, mybir.dt.float32, kind="ExternalOutput").ap()
    gnn_residual_layernorm(nc, *args, out)
    r = run_bass_kernel_spmd(nc, [arrays], core_ids=[0])
    return r.results[0]["out_dram"]
```
